# Optimizing a Trainium2 kernel written in Bass

```python
import numpy as np
import jax
import jax.numpy as jnp

def _softmax(x, axis=-1):
    return jax.nn.softmax(x, axis=axis)

def _gelu(x):
    return jax.nn.gelu(x, approximate=True)

def _silu(x):
    return jax.nn.silu(x)

def _sigmoid(x):
    return jax.nn.sigmoid(x)

def _layernorm(x, axis=-1, eps=1e-05):
    m = jnp.mean(x, axis=axis, keepdims=True)
    v = jnp.var(x, axis=axis, keepdims=True)
    return (x - m) / jnp.sqrt(v + eps)

def _scatter_add(tgt, idx, src, axis=0):
    return tgt.at[idx].add(src)

def _segment_sum(src, seg, n):
    return jax.ops.segment_sum(src, seg, n)
kernel_name = 'mk_adaln_ffn_d1_seqx_r4_7113fd'

def setup_inputs(seed: int=0):
    np.random.seed(seed)
    _w = jnp.asarray

    def _rec_inputs():
        import jax
        import jax.numpy as jnp
        _rk = jax.random.key(seed)
        x = -0.000125 + 0.9999 * jax.random.normal(jax.random.fold_in(_rk, 1), (128, 64, 256), jnp.float32)
        _lenS = 64 - jax.random.randint(jax.random.fold_in(_rk, 7), (128,), 0, max(1, 64 // 4) + 1, jnp.int32)
        _lenS2 = 64 - jax.random.randint(jax.random.fold_in(_rk, 8), (128,), 0, max(1, 64 // 4) + 1, jnp.int32)
        cond_1024 = -0.00493535 + 1.00056 * jax.random.normal(jax.random.fold_in(_rk, 11), (128, 256), jnp.float32)
        return (x, cond_1024)
    x, cond_1024 = _rec_inputs()

    def _L0_cond_setup():
        import jax, jax.numpy as jnp
        import numpy as np
        import math
        N, T, D, H = (64, 128, 256, 256)
        key = jax.random.key(seed)
        k1, k2, k3, k4 = jax.random.split(key, 4)
        x = jax.random.normal(k1, (N, T, D), dtype=jnp.float32)
        h0 = jax.random.normal(k2, (N, H), dtype=jnp.float32)
        Wx = jax.random.normal(k3, (D, H), dtype=jnp.float32) / math.sqrt(D)
        Wh = jax.random.normal(k4, (H, H), dtype=jnp.float32) / math.sqrt(H)
        b = jnp.zeros((H,), dtype=jnp.float32)
        return {'x': x, 'h0': h0, 'Wx': Wx, 'Wh': Wh, 'b': b}
    _L0_cond_all = _L0_cond_setup()
    _L0_cond_in = {k: v for k, v in _L0_cond_all.items() if k in ('Wx', 'Wh', 'b')}
    del _L0_cond_all

    def _L0_ffn_setup():
        import jax, jax.numpy as jnp
        import numpy as np
        B, S, D, E = (2, 512, 256, 8)
        key = jax.random.key(seed)
        ks = jax.random.split(key, 5)
        x = jax.random.normal(ks[0], (B, S, D), dtype=jnp.float32)
        router_w = jax.random.normal(ks[1], (E, D), dtype=jnp.float32) * 0.02
        router_b = jnp.zeros((E,), dtype=jnp.float32)
        expert_w = jax.random.normal(ks[2], (E, D, D), dtype=jnp.float32) * 0.02
        expert_b = jnp.zeros((E, D), dtype=jnp.float32)
        return {'x': x, 'router_w': router_w, 'router_b': router_b, 'expert_w': expert_w, 'expert_b': expert_b}
    _L0_ffn_all = _L0_ffn_setup()
    _L0_ffn_in = {k: v for k, v in _L0_ffn_all.items() if k in ('router_w', 'router_b', 'expert_w', 'expert_b')}
    del _L0_ffn_all
    return {'x': x, 'cond_1024': cond_1024, 'L0_cond_Wx': _L0_cond_in['Wx'], 'L0_cond_Wh': _L0_cond_in['Wh'], 'L0_cond_b': _L0_cond_in['b'], 'L0_ffn_router_w': _L0_ffn_in['router_w'], 'L0_ffn_router_b': _L0_ffn_in['router_b'], 'L0_ffn_expert_w': _L0_ffn_in['expert_w'], 'L0_ffn_expert_b': _L0_ffn_in['expert_b']}

def reference(x, cond_1024, L0_cond_Wx, L0_cond_Wh, L0_cond_b, L0_ffn_router_w, L0_ffn_router_b, L0_ffn_expert_w, L0_ffn_expert_b):
    import jax
    import jax.numpy as jnp

    def _L0_cond_ref(x, h0, Wx, Wh, b):
        import jax, jax.numpy as jnp
        import numpy as np
        import math
        N, T, D, H = (64, 128, 256, 256)
        xW = jnp.einsum('ntd,dh->nth', x, Wx) + b

        def step(prev_h, xw_t):
            next_h = jnp.tanh(prev_h @ Wh + xw_t)
            return (next_h, next_h)
        _, hs = jax.lax.scan(step, h0, jnp.swapaxes(xW, 0, 1))
        return jnp.swapaxes(hs, 0, 1)

    def _L0_ffn_ref(x, router_w, router_b, expert_w, expert_b):
        import jax, jax.numpy as jnp
        import numpy as np
        B, S, D, E = (2, 512, 256, 8)
        logits = jnp.einsum('bsd,ed->bse', x, router_w) + router_b
        probs = jax.nn.softmax(logits, axis=-1)
        weights = jnp.max(probs, axis=-1)
        top1 = jnp.argmax(probs, axis=-1)
        y_all = jnp.einsum('bsd,eod->bseo', x, expert_w) + expert_b
        y = jnp.take_along_axis(y_all, top1[:, :, None, None], axis=2)[:, :, 0, :]
        out = y * weights[:, :, None]
        return out
    x = x + _L0_ffn_ref(_L0_cond_ref(x, cond_1024, L0_cond_Wx, L0_cond_Wh, L0_cond_b), L0_ffn_router_w, L0_ffn_router_b, L0_ffn_expert_w, L0_ffn_expert_b)
    return x

_drawn_inputs = setup_inputs


def setup_inputs(seed=0):
    import zlib

    import numpy as np

    out = dict(_drawn_inputs(seed))
    spreads = {'L0_cond_b': (0.0, 0.426),
     'L0_ffn_router_b': (0.0, 0.286),
     'L0_ffn_expert_b': (0.0, 0.457)}
    factors = {'cond_1024': 7.126}
    for name, (base, spread) in spreads.items():
        noise = np.random.default_rng([zlib.crc32(name.encode()), seed]).standard_normal(out[name].shape)
        drawn = base * np.exp(spread * noise) if base else spread * noise
        out[name] = jnp.asarray(drawn.astype(out[name].dtype))
    for name, factor in factors.items():
        out[name] = (out[name] * factor).astype(out[name].dtype)
    return out
```

```python
from contextlib import ExitStack

import concourse.bass as bass
from concourse import mybir

F32 = mybir.dt.float32
F32R = mybir.dt.float32r
BF16 = mybir.dt.bfloat16
U32 = mybir.dt.uint32
ALU = mybir.AluOpType
ACT = mybir.ActivationFunctionType
AX = mybir.AxisListType

P = 128
T = 64
D = 256
KC = D // P
E = 8
NTOK = P * T
GS = 4
NG = T // GS
GW = GS * P
NB = 4
NI = NG // NB
CAP = NTOK + P
FILL0 = E * CAP
ROWS = FILL0 + P
LW = P + E
COL_L, COL_H1, COL_X = P, LW, LW + P
COL_W, COL_ID = COL_X + D, COL_X + D + 1
RW = 2 * D + 16
NT = NTOK // P + E
ROUND = 8388608.0
RB = 8
RP = 4


def later(i):
    return not (isinstance(i, int) and i == 0)


def adaln_moe_kernel(nc, xT, x, cT, Wx, Wh, b, rwT, rb, weT, be, out):
    ctx = ExitStack()
    with ctx:
        def sb(name, shape, dt=F32):
            return ctx.enter_context(nc.sbuf_tensor(name, shape, dt))

        def ps(name, shape, dt=F32):
            return ctx.enter_context(nc.psum_tensor(name, shape, dt))

        def sem(name):
            return ctx.enter_context(nc.semaphore(name))

        srt = nc.dram_tensor("sorted_rows", [ROWS, RW], F32).ap()
        out_rows = out.rearrange("n t d -> (n t) d")

        wx = sb("wx", [P, KC, D])
        wx_hi = sb("wx_hi", [P, KC, D], F32R)
        wx_lo = sb("wx_lo", [P, KC, D], F32R)
        wh = sb("wh", [P, KC, D])
        bias = sb("bias", [P, KC])
        idr = sb("idr", [P, 2 * LW])
        rb_bc = sb("rb_bc", [P, GS, E])
        we = sb("we", [P, KC, E * D])
        we_hi = [sb(f"we_hi{k}", [P, E * D], F32R) for k in range(KC)]
        we_lo = [sb(f"we_lo{k}", [P, E * D], F32R) for k in range(KC)]
        be2 = sb("be2", [2, E * D])
        be_hi = sb("be_hi", [2, E * D], F32R)
        be_t = sb("be_t", [2, E * D])
        be_parts = sb("be_parts", [2, E * D], F32R)
        ones2 = sb("ones2", [2, P], F32R)
        tri = sb("tri", [P, P], BF16)
        ones = sb("ones", [P, P], BF16)
        e_m8 = sb("e_m8", [P, GS, E])
        e_cap = sb("e_cap", [P, GS, E])
        pid = sb("pid", [P, 1])
        tile_row = sb("tile_row", [P, E])
        sgn = sb("sgn", [2, 1])
        ids = sb("ids", [P, T], U32)

        xg = [sb(f"xg{i}", [P, KC, GW]) for i in range(2)]
        x_hi = [sb(f"x_hi{i}", [P, KC, GW], F32R) for i in range(2)]
        x_lo = [sb(f"x_lo{i}", [P, KC, GW], F32R) for i in range(2)]
        h0 = sb("h0", [P, KC, P])
        hT = [sb(f"hT{i}", [P, KC, P]) for i in range(GS)]
        rows = [sb(f"rows{i}", [P, GS, RW]) for i in range(NB)]
        lg = sb("lg", [P, GS, E])
        mx = sb("mx", [P, GS])
        dl = sb("dl", [P, GS, E])
        ex = sb("ex", [P, GS, E])
        sm = sb("sm", [P, GS])
        sf = sb("sf", [P, GS])
        ea = sb("ea", [P, GS, E])
        ei = sb("ei", [P, GS])
        oh = sb("oh", [P, GS, E], BF16)
        cum = [sb(f"cum{i}", [P, GS, E], BF16) for i in range(2)]
        rk = sb("rk", [P, GS, E])
        rs = sb("rs", [P, GS, E])
        slot = [sb(f"slot{i}", [P, GS], U32) for i in range(NB)]

        filler = sb("filler", [P, RW])
        fill_at = sb("fill_at", [1, E], U32)
        frac = sb("frac", [P, E])
        scan = [sb(f"scan{i}", [P, E // 2 + E]) for i in range(4)]
        cex = sb("cex", [P, E])
        inl = sb("inl", [P, E])
        inr = sb("inr", [P, E])
        at_row = sb("at_row", [P, E])
        prod = sb("prod", [P, E])
        tc = [sb(f"tc{i}", [P, 1]) for i in range(4)]
        tab = sb("tab", [1, 2, P], U32)

        tile_in = [sb(f"tile_in{i}", [P, RW]) for i in range(RB)]
        tile_id = [sb(f"tile_id{i}", [P, 1], U32) for i in range(RB)]
        tile_out = [sb(f"tile_out{i}", [P, D]) for i in range(RB)]
        hs_hi = [sb(f"hs_hi{i}", [P, KC, P], F32R) for i in range(RP)]
        hs_lo = [sb(f"hs_lo{i}", [P, KC, P], F32R) for i in range(RP)]

        pre = [[ps(f"pre{i}{j}", [P, GW]) for j in range(KC)] for i in range(2)]
        ptr = [ps(f"ptr{i}", [P, 512]) for i in range(2)]
        pcn = ps("pcn", [P, 512])
        prk = ps("prk", [P, 512])
        p_rank = prk[:, 0:GS * E].rearrange("p (s e) -> p s e", s=GS)
        p_cnt = pcn[:, 64:64 + E]
        p_tab = pcn[0:1, 128:128 + 2 * P].rearrange("p (a n) -> p a n", a=2)
        py = [pre[0][0], pre[0][1], pre[1][0], pre[1][1]]
        pt2 = [ptr[0], ptr[1], pcn, prk]

        wx_in = sem("wx_in")
        wh_in = sem("wh_in")
        b_in = sem("b_in")
        r_in = sem("r_in")
        be_in = sem("be_in")
        we_in = sem("we_in")
        xg_in = [sem(f"xg_in{i}") for i in range(2)]
        xn_in = [sem(f"xn_in{i}") for i in range(NB)]
        consts = sem("consts")
        g_chain = sem("g_chain")
        pool_go = sem("pool_go")
        v_chain = sem("v_chain")
        w_ready = sem("w_ready")
        split_ready = sem("split_ready")
        wx_done = sem("wx_done")
        pre_ready = sem("pre_ready")
        h_ready = sem("h_ready")
        tr_ready = sem("tr_ready")
        hn_ready = sem("hn_ready")
        d_ready = sem("d_ready")
        e_ready = sem("e_ready")
        oh_ready = sem("oh_ready")
        rank_ready = sem("rank_ready")
        slots_ready = sem("slots_ready")
        scat = [sem(f"scat{i}") for i in range(NB)]
        cum_last = sem("cum_last")
        cnt_ready = sem("cnt_ready")
        fill_ready = sem("fill_ready")
        filled = [sem(f"filled{i}") for i in range(E + 1)]
        hi_ready = sem("hi_ready")
        h_chain = sem("h_chain")
        tabc_ready = sem("tabc_ready")
        tabp_ready = sem("tabp_ready")
        tab_ready = sem("tab_ready")
        t_in = [sem(f"t_in{i}") for i in range(RB)]
        t_tr = [sem(f"t_tr{i}") for i in range(RP)]
        t_hi = [sem(f"t_hi{i}") for i in range(RP)]
        t_lo = [sem(f"t_lo{i}") for i in range(RP)]
        t_y = [sem(f"t_y{i}") for i in range(RP)]
        t_o = [sem(f"t_o{i}") for i in range(RB)]
        t_out = [sem(f"t_out{i}") for i in range(RB)]

        block = ctx.enter_context(nc.Block())

        def column(eng, n, i, most):
            return nc.values_load_multi_w_load_instructions(
                tab[0:1, n, bass.ds(i * RB, RB)], engines=[eng.engine], min_val=0, max_val=most,
                skip_runtime_bounds_check_because="the table holds nothing else")[1]

        def fill_behind(eng, first):
            eng.wait_ge(fill_ready, 1)
            for e in range(first, E, 2):
                start = eng.value_load(fill_at[0:1, e:e + 1], min_val=0, max_val=FILL0 - P)
                eng.dma_start(srt[bass.ds(start, P), :], filler[:, :]).then_inc(filled[e], 16)

        @block.sync
        def _(sp):
            def load_group(i, bs):
                if later(i) or bs > 1:
                    sp.wait_ge(split_ready, NB * i + bs - 1)
                sp.dma_start(xg[bs % 2][:, :, :].rearrange("p k n -> p (k n)"),
                             xT[NB * i + bs, :, :]).then_inc(xg_in[bs % 2], 16)

            def load_rows(i, bs):
                if later(i):
                    sp.wait_ge(scat[bs], i * (16 * GS))
                sp.dma_start(rows[bs][:, :, COL_X:COL_X + D],
                             x[:, bass.ds((NB * i + bs) * GS, GS), :]).then_inc(xn_in[bs], 16)

            sp.dma_start(wx[:, :, :].rearrange("p k n -> p (k n)"), Wx).then_inc(wx_in, 16)
            load_group(0, 0)
            sp.dma_start(h0[:, :, :].rearrange("p k n -> p (k n)"), cT).then_inc(wh_in, 16)
            load_group(0, 1)
            load_rows(0, 0)

            def body(i):
                for bs in range(0 if later(i) else 2, NB):
                    load_group(i, bs)
                    load_rows(*((i, bs - 1) if bs else (i - 1, NB - 1)))

            body(0)
            sp.wait_ge(consts, 1)
            sp.dma_start(srt[FILL0:ROWS, :], filler[:, :]).then_inc(filled[E], 16)
            with sp.Fori(1, NI) as i:
                body(i)
            load_rows(NI - 1, NB - 1)

            fill_behind(sp, 0)
            sp.wait_ge(tab_ready, 1)
            for bs in range(NB):
                sp.wait_ge(scat[bs], NI * 16 * GS)
            for e in range(E + 1):
                sp.wait_ge(filled[e], 16)

            def tiles(i):
                starts = column(sp, 0, i, ROWS - P)
                for q in range(RB):
                    if later(i):
                        sp.wait_ge(t_o[q], i)
                    sp.dma_start(tile_in[q][:, :], srt[bass.ds(starts[q], P), :]).then_inc(t_in[q], 16)

            tiles(0)
            with sp.Fori(1, NT // RB) as i:
                tiles(i)

        @block.gpsimd
        def _(pool):
            pool.memset(idr[:, 0:P], 0.0).then_inc(g_chain, 1)
            pool.memset(idr[:, 2 * LW - P:2 * LW], 0.0).then_inc(g_chain, 1)
            pool.memset(tri[:, :], 1.0).then_inc(g_chain, 1)
            pool.memset(filler[:, :], 0.0).then_inc(g_chain, 1)
            pool.memset(ones[:, :], 1.0)
            pool.memset(ones2[:, :].bitcast(F32), 1.0)
            pool.memset(cum[0][:, 0, :], 0.0)
            for bs in range(NB):
                pool.memset(rows[bs][:, :, COL_ID + 1:RW], 0.0)
            pool.iota(e_m8[:, :, :], pattern=[[0, GS], [1, E]], base=-E, channel_multiplier=0,
                      allow_small_or_imprecise_dtypes=True)
            pool.iota(e_cap[:, :, :], pattern=[[0, GS], [CAP, E]], base=0, channel_multiplier=0,
                      allow_small_or_imprecise_dtypes=True)
            pool.iota(pid[:, :], pattern=[[0, 1]], base=0, channel_multiplier=1,
                      allow_small_or_imprecise_dtypes=True)
            pool.iota(sgn[:, :], pattern=[[0, 1]], base=1, channel_multiplier=-2,
                      allow_small_or_imprecise_dtypes=True)
            pool.iota(tile_row[:, :], pattern=[[CAP, E]], base=-FILL0, channel_multiplier=P,
                      allow_small_or_imprecise_dtypes=True)
            for a in scan:
                pool.memset(a[:, 0:E // 2], 0.0)
            pool.iota(ids[:, :], pattern=[[1, T]], base=0, channel_multiplier=T)
            pool.wait_ge(g_chain, 4)
            pool.iota(filler[:, COL_ID:COL_ID + 1].bitcast(U32), pattern=[[0, 1]], base=NTOK, channel_multiplier=0)
            for at in (0, 2 * LW - P):
                pool.affine_select(out=idr[:, at:at + P], in_=idr[:, at:at + P], compare_op=ALU.not_equal, fill=1.0,
                                   base=0, pattern=[[-1, P]], channel_multiplier=1)
            pool.affine_select(out=tri[:, :], in_=tri[:, :], compare_op=ALU.is_gt, fill=0.0,
                               base=0, pattern=[[1, P]], channel_multiplier=-1).then_inc(consts, 1)

            with pool.Fori(0, NI) as i:
                for bs in range(NB):
                    pool.wait_ge(slots_ready, NB * i + bs + 1)
                    pool.wait_ge(hn_ready, (NB * i + bs + 1) * GS)
                    pool.wait_ge(xn_in[bs], i * 16 + 16)
                    pool.sem_inc(pool_go, 1)
                    for s in range(GS):
                        pool.indirect_dma_start(
                            out=srt[:, :], out_offset=bass.IndirectOffsetOnAxis(ap=slot[bs][:, s:s + 1], axis=0),
                            in_=rows[bs][:, s, :], in_offset=None).then_inc(scat[bs], 16)

            last_token = pool.to_reg(NTOK - 1)
            with pool.Fori(0, NT // RB) as i:
                for q in range(RB):
                    pool.wait_ge(t_o[q], i + 1)
                    pool.sem_inc(pool_go, 1)
                    pool.indirect_dma_start(
                        out=out_rows, out_offset=bass.IndirectOffsetOnAxis(ap=tile_id[q][:, 0:1], axis=0),
                        in_=tile_out[q][:, :], in_offset=None,
                        bounds_check=last_token, oob_is_err=False).then_inc(t_out[q], 16)
            for q in range(RB):
                pool.wait_ge(t_out[q], 16 * (NT // RB))

        @block.scalar
        def _(act):
            act.dma_start(wh[:, :, :].rearrange("p k n -> p (k n)"), Wh).then_inc(wh_in, 16)
            act.dma_start(bias[:, :], b).then_inc(b_in, 16)
            act.dma_start(idr[:, P:P + KC * E], rwT).then_inc(r_in, 16)
            act.dma_start(rb_bc[:, :, :], bass.AP(tensor=rb.tensor, offset=rb.offset,
                                                  ap=[[0, P], [0, GS], [1, E]])).then_inc(r_in, 16)
            act.dma_start(be2[:, :], bass.AP(tensor=be.tensor, offset=be.offset,
                                             ap=[[0, 2], [1, E * D]])).then_inc(be_in, 16)
            act.dma_start(we[:, :, :].rearrange("p k m -> p (k m)"), weT).then_inc(we_in, 16)
            act.wait_ge(b_in, 16)

            def tanh(i, bs, s):
                t = NB * GS * i + GS * bs + s
                for j in range(KC):
                    act.wait_ge(pre_ready, KC * t + j + 1)
                    nc.scalar.activation(hT[s][:, j, :], pre[bs % 2][j][:, s * P:(s + 1) * P], ACT.Tanh,
                                         bias=bias[:, j:j + 1]).then_inc(h_ready, 1)

            def store_h(i, bs, s):
                t = NB * GS * i + GS * bs + s
                if s == 0 and later(i):
                    act.wait_ge(scat[bs], i * (16 * GS))
                act.wait_ge(tr_ready, t + 1)
                nc.scalar.copy(rows[bs][:, s, 0:COL_X], ptr[s % 2][:, 0:COL_X]).then_inc(hn_ready, 1)

            def exps(i, bs):
                act.wait_ge(d_ready, NB * i + bs + 1)
                nc.scalar.activation(ex[:, :, :], dl[:, :, :], ACT.Exp).then_inc(e_ready, 1)

            def body(i):
                for bs in range(NB):
                    last = (i, bs - 1) if bs else (i - 1, NB - 1)
                    for s in range(GS):
                        tanh(i, bs, s)
                        if s:
                            store_h(i, bs, s - 1)
                        elif bs or later(i):
                            store_h(*last, GS - 1)
                        if s == 1 and (bs or later(i)):
                            exps(*last)

            body(0)
            with act.Fori(1, NI) as i:
                body(i)
            store_h(NI - 1, NB - 1, GS - 1)
            exps(NI - 1, NB - 1)
            fill_behind(act, 1)

            def tiles(i):
                for q in range(RB):
                    qp, n = q % RP, RB // RP * i + q // RP
                    act.wait_ge(t_tr[qp], n + 1)
                    if q >= RP or later(i):
                        act.wait_ge(t_y[qp], n)
                    nc.scalar.copy(hs_hi[qp][:, :, :].rearrange("p k n -> p (k n)"), pt2[qp][:, 0:D]).then_inc(t_hi[qp], 1)

            tiles(0)
            with act.Fori(1, NT // RB) as i:
                tiles(i)

        WE_PARTS = 4
        CHOOSE = 8
        RK = CHOOSE + 3

        @block.vector
        def _(dve):
            V = nc.vector

            dve.wait_ge(wx_in, 16)
            V.tensor_copy(wx_hi[:, :, :], wx[:, :, :]).then_inc(w_ready, 1)
            dve.wait_ge(w_ready, 1)
            V.tensor_tensor(wx_lo[:, :, :], wx[:, :, :], wx_hi[:, :, :].bitcast(F32), ALU.subtract).then_inc(w_ready, 1)

            def split(i, bs):
                g = NB * i + bs
                ring = bs % 2
                dve.wait_ge(xg_in[ring], (NB // 2 * i + bs // 2 + 1) * 16)
                if later(i) or bs > 1:
                    dve.wait_ge(wx_done, g - 1)
                V.tensor_copy(x_hi[ring][:, :, :], xg[ring][:, :, :]).then_inc(hi_ready, 1)
                dve.wait_ge(hi_ready, g + 1)
                V.tensor_tensor(x_lo[ring][:, :, :], xg[ring][:, :, :], x_hi[ring][:, :, :].bitcast(F32),
                                ALU.subtract).then_inc(split_ready, 1)

            def route_choose(i, bs):
                g = NB * i + bs
                c = RK * g

                def over_e(a):
                    return a[:, :].rearrange("p (s o) -> p s o", o=1).to_broadcast([P, GS, E])

                dve.wait_ge(hn_ready, (g + 1) * GS)
                V.tensor_tensor(lg[:, :, :], rows[bs][:, :, COL_L:COL_L + E], rb_bc[:, :, :], ALU.add).then_inc(v_chain, 1)
                dve.wait_ge(v_chain, c + 1)
                V.reduce_max(mx[:, :], lg[:, :, :], AX.X).then_inc(v_chain, 1)
                dve.wait_ge(v_chain, c + 2)
                V.tensor_tensor(dl[:, :, :], lg[:, :, :], over_e(mx), ALU.subtract).then_inc(d_ready, 1)
                dve.wait_ge(d_ready, g + 1)
                V.scalar_tensor_tensor(out=ea[:, :, :], in0=dl[:, :, :], scalar=0.0, in1=e_m8[:, :, :],
                                       op0=ALU.is_ge, op1=ALU.mult).then_inc(v_chain, 1)
                dve.wait_ge(v_chain, c + 3)
                V.tensor_reduce(ei[:, :], ea[:, :, :], AX.X, ALU.min).then_inc(v_chain, 1)
                dve.wait_ge(v_chain, c + 4)
                V.tensor_tensor(oh[:, :, :], e_m8[:, :, :], over_e(ei), ALU.is_equal).then_inc(v_chain, 1)
                dve.wait_ge(v_chain, c + 5)
                for s in range(1, GS):
                    add = V.tensor_tensor(cum[bs % 2][:, s, :], cum[bs % 2][:, s - 1, :], oh[:, s - 1, :], ALU.add)
                    if s < GS - 1:
                        add.then_inc(v_chain, 1)
                        dve.wait_ge(v_chain, c + 5 + s)
                    else:
                        add.then_inc(oh_ready, 1)
                        dve.wait_ge(oh_ready, g + 1)
                V.tensor_tensor(cum[1 - bs % 2][:, 0, :], cum[bs % 2][:, GS - 1, :], oh[:, GS - 1, :],
                                ALU.add).then_inc(v_chain, 1)

            def route_place(i, bs):
                g = NB * i + bs
                c = RK * g + CHOOSE
                dve.wait_ge(rank_ready, g + 1)
                V.tensor_tensor(rk[:, :, :], p_rank, e_cap[:, :, :], ALU.add).then_inc(v_chain, 1)
                dve.wait_ge(v_chain, c + 1)
                V.tensor_tensor(rs[:, :, :], rk[:, :, :], oh[:, :, :], ALU.mult).then_inc(v_chain, 1)
                dve.wait_ge(v_chain, c + 2)
                V.reduce_sum(sf[:, :], rs[:, :, :], AX.X)
                dve.wait_ge(e_ready, g + 1)
                V.reduce_sum(sm[:, :], ex[:, :, :], AX.X).then_inc(v_chain, 1)
                dve.wait_ge(v_chain, c + 3)
                if later(i):
                    dve.wait_ge(scat[bs], i * (16 * GS))
                V.tensor_copy(slot[bs][:, :], sf[:, :])
                V.reciprocal(rows[bs][:, :, COL_W], sm[:, :])
                V.tensor_copy(rows[bs][:, :, COL_ID].bitcast(U32), ids[:, bass.ds(g * GS, GS)]).then_inc(slots_ready, 1)

            def body(i, last=False):
                for bs in range(NB):
                    if bs or later(i):
                        before = (i, bs - 1) if bs else (i - 1, NB - 1)
                        route_choose(*before)
                        route_place(*before)
                    if not later(i):
                        split_experts(bs)
                    if bs < NB - 2:
                        split(i, bs + 2)
                    elif not last:
                        split(i + 1, bs + 2 - NB)

            def split_experts(part):
                if part == 0:
                    dve.wait_ge(be_in, 16)
                    dve.wait_ge(consts, 1)
                    V.tensor_copy(be_hi[:, :], be2[:, :])
                    V.tensor_scalar(be_t[:, :], be2[:, :], pid[0:2, 0:1], None, ALU.mult).then_inc(w_ready, 1)
                    dve.wait_ge(w_ready, 3)
                    V.scalar_tensor_tensor(out=be_parts[:, :], in0=be_hi[:, :].bitcast(F32), scalar=sgn[:, 0:1],
                                           in1=be_t[:, :], op0=ALU.mult, op1=ALU.add)
                else:
                    dve.wait_ge(we_in, 16)
                    for n in range(WE_PARTS * (part - 1) // (NB - 1), WE_PARTS * part // (NB - 1)):
                        k, at = divmod(n * (KC * E * D // WE_PARTS), E * D)
                        cols = slice(at, at + KC * E * D // WE_PARTS)
                        V.tensor_copy(we_hi[k][:, cols], we[:, k, cols]).then_inc(w_ready, 1)
                        dve.wait_ge(w_ready, 4 + n)
                        V.tensor_tensor(we_lo[k][:, cols], we[:, k, cols], we_hi[k][:, cols].bitcast(F32), ALU.subtract)

            split(0, 0)
            split(0, 1)
            dve.wait_ge(r_in, 32)
            body(0)
            with dve.Fori(1, NI - 1) as i:
                body(i)
            body(NI - 1, last=True)
            route_choose(NI - 1, NB - 1)
            route_place(NI - 1, NB - 1)

            dve.wait_ge(cnt_ready, 1)
            V.tensor_tensor(fill_at[:, :], p_cnt[0:1, :], e_cap[0:1, 0, :], ALU.add).then_inc(fill_ready, 1)

            chain = [0]

            def link(ins):
                chain[0] += 1
                ins.then_inc(h_chain, 1)
                dve.wait_ge(h_chain, chain[0])

            H = E // 2
            whole = [a[:, H:H + E] for a in scan]
            link(V.tensor_scalar(frac[:, :], p_cnt, 1.0 / P, (P - 1) / (2.0 * P), ALU.mult, ALU.add))
            link(V.tensor_scalar(whole[0], frac[:, :], ROUND, ROUND, ALU.add, ALU.subtract))
            for n in range(3):
                link(V.tensor_tensor(whole[n + 1], whole[n], scan[n][:, H - (1 << n):H - (1 << n) + E], ALU.add))
            cin = whole[3]
            V.tensor_scalar(inl[:, :], cin, pid[:, 0:1], None, ALU.is_le)
            link(V.tensor_tensor(cex[:, :], cin, whole[0], ALU.subtract))
            V.reduce_sum(tc[1][:, :], inl[:, :], AX.X)
            V.scalar_tensor_tensor(out=inr[:, :], in0=cex[:, :], scalar=pid[:, 0:1], in1=inl[:, :],
                                   op0=ALU.is_le, op1=ALU.subtract)
            link(V.scalar_tensor_tensor(out=at_row[:, :], in0=cex[:, :], scalar=float(-P), in1=tile_row[:, :],
                                        op0=ALU.mult, op1=ALU.add))
            V.tensor_scalar(tc[3][:, :], tc[1][:, :], float(E - 1), float(D), ALU.min, ALU.mult)
            link(V.tensor_tensor(prod[:, :], at_row[:, :], inr[:, :], ALU.mult))
            link(V.reduce_sum(tc[0][:, :], prod[:, :], AX.X))
            V.tensor_scalar(tc[2][:, :], tc[0][:, :], float(FILL0), None, ALU.add).then_inc(tabc_ready, 1)
            dve.wait_ge(tabp_ready, 1)
            V.tensor_copy(tab[:, :, :], p_tab).then_inc(tab_ready, 1)

            def low_parts(i, q):
                qp, n = q % RP, RB // RP * i + q // RP
                if q >= RP or later(i):
                    dve.wait_ge(t_y[qp], n)
                dve.wait_ge(t_hi[qp], n + 1)
                V.tensor_tensor(hs_lo[qp][:, :, :].rearrange("p k n -> p (k n)"), pt2[qp][:, 0:D],
                                hs_hi[qp][:, :, :].rearrange("p k n -> p (k n)").bitcast(F32),
                                ALU.subtract).then_inc(t_lo[qp], 1)

            def tiles(i):
                low_parts(i, 0)
                for q in range(RB):
                    if q + 1 < RB:
                        low_parts(i, q + 1)
                    qp, n = q % RP, RB // RP * i + q // RP
                    if later(i):
                        dve.wait_ge(t_out[q], i * 16)
                    dve.wait_ge(t_y[qp], n + 1)
                    V.tensor_copy(tile_id[q][:, :], tile_in[q][:, COL_ID:COL_ID + 1].bitcast(U32))
                    V.scalar_tensor_tensor(out=tile_out[q][:, :], in0=py[qp][:, 0:D],
                                           scalar=tile_in[q][:, COL_W:COL_W + 1],
                                           in1=tile_in[q][:, COL_X:COL_X + D],
                                           op0=ALU.mult, op1=ALU.add).then_inc(t_o[q], 1)

            tiles(0)
            with dve.Fori(1, NT // RB) as i:
                tiles(i)

        @block.tensor
        def _(pe):
            mm = nc.tensor.matmul

            def project(ring, s):
                j, k = s // KC, s % KC
                cols = slice(j * P, (j + 1) * P)
                mm(pre[ring][j][:, :], wx_hi[:, k, cols], x_hi[ring][:, k, :], start=(k == 0), stop=False, skip_group_check=True)
                mm(pre[ring][j][:, :], wx_lo[:, k, cols], x_hi[ring][:, k, :], start=False, stop=False, skip_group_check=True)
                last = mm(pre[ring][j][:, :], wx_hi[:, k, cols], x_lo[ring][:, k, :], start=False, stop=False, skip_group_check=True)
                if s == GS - 1:
                    last.then_inc(wx_done, 1)

            def recur(i, bs, s, first=False):
                t = NB * GS * i + GS * bs + s
                old = h0 if first else hT[(s - 1) % GS]
                for j in range(KC):
                    for k in range(KC):
                        if j == 0 and not first:
                            pe.wait_ge(h_ready, KC * t - 1 + k)
                        last = mm(pre[bs % 2][j][:, s * P:(s + 1) * P], wh[:, k, j * P:(j + 1) * P], old[:, k, :],
                                  start=False, stop=(k == KC - 1), skip_group_check=True)
                    last.then_inc(pre_ready, 1)

            def after(i, bs, s):
                t = NB * GS * i + GS * bs + s
                if later(i) or bs or s > 1:
                    pe.wait_ge(hn_ready, t - 1)
                for k in range(KC):
                    last = mm(ptr[s % 2][:, k * P:k * P + LW], hT[s][:, k, :], idr[:, k * LW:(k + 1) * LW],
                              start=(k == 0), stop=(k == KC - 1), skip_group_check=True)
                last.then_inc(tr_ready, 1)

            def rank(i, bs):
                pe.wait_ge(oh_ready, NB * i + bs + 1)
                mm(p_rank, tri[:, :], oh[:, :, :], start=True, stop=False, skip_group_check=True)
                mm(p_rank, ones[:, :], cum[bs % 2][:, :, :], start=False, stop=True, skip_group_check=True).then_inc(rank_ready, 1)

            def body(i, last=False):
                for bs in range(NB):
                    before = (i, bs - 1) if bs else (i - 1, NB - 1)
                    started = bs > 0 or later(i)
                    for s in range(GS):
                        recur(i, bs, s, first=not started and s == 0)
                        if s:
                            after(i, bs, s - 1)
                        elif started:
                            after(*before, GS - 1)
                        if not (last and bs == NB - 1):
                            if s == 0:
                                pe.wait_ge(split_ready, NB * i + bs + 2)
                            project(1 - bs % 2, s)
                        if s == 1 and started:
                            rank(*before)

            pe.wait_ge(w_ready, 2)
            pe.wait_ge(split_ready, 1)
            for s in range(GS):
                project(0, s)
            pe.wait_ge(wh_in, 32)
            pe.wait_ge(consts, 1)
            pe.wait_ge(r_in, 32)
            body(0)
            with pe.Fori(1, NI - 1) as i:
                body(i)
            body(NI - 1, last=True)
            pe.wait_ge(h_ready, KC * T)
            after(NI - 1, NB - 1, GS - 1)
            rank(NI - 1, NB - 1)
            pe.wait_ge(v_chain, RK * (NG - 1) + CHOOSE)
            mm(p_cnt, ones[:, :], cum[0][:, 0, :], start=True, stop=True, skip_group_check=True).then_inc(cnt_ready, 1)
            pe.wait_ge(tabc_ready, 1)
            mm(p_tab[:, 0, :], tc[2][:, :], idr[:, 0:P], start=True, stop=True, skip_group_check=True)
            mm(p_tab[:, 1, :], tc[3][:, :], idr[:, 0:P], start=True, stop=True,
               skip_group_check=True).then_inc(tabp_ready, 1)

            pe.wait_ge(tab_ready, 1)
            pe.wait_ge(hn_ready, T)

            def turn(i, q):
                qp, n = q % RP, RB // RP * i + q // RP
                pe.wait_ge(t_in[q], i * 16 + 16)
                if q >= RP or later(i):
                    pe.wait_ge(t_lo[qp], n)
                for k in range(KC):
                    last = nc.tensor.transpose(pt2[qp][:, k * P:(k + 1) * P], tile_in[q][:, k * LW:k * LW + P], idr[:, 0:P])
                last.then_inc(t_tr[qp], 1)

            def product(i, q, at):
                qp, n = q % RP, RB // RP * i + q // RP
                cols = bass.ds(at, D)
                if q >= RP:
                    pe.wait_ge(t_o[q - RP], i + 1)
                elif later(i):
                    pe.wait_ge(t_o[q + RP], i)
                mm(py[qp][:, 0:D], ones2[:, :], be_parts[:, cols], start=True, stop=False, skip_group_check=True)
                pe.wait_ge(t_hi[qp], n + 1)
                for k in range(KC):
                    mm(py[qp][:, 0:D], hs_hi[qp][:, k, :], we_hi[k][:, cols], start=False, stop=False, skip_group_check=True)
                    mm(py[qp][:, 0:D], hs_hi[qp][:, k, :], we_lo[k][:, cols], start=False, stop=False, skip_group_check=True)
                pe.wait_ge(t_lo[qp], n + 1)
                for k in range(KC):
                    last = mm(py[qp][:, 0:D], hs_lo[qp][:, k, :], we_hi[k][:, cols], start=False, stop=(k == KC - 1),
                              skip_group_check=True)
                last.then_inc(t_y[qp], 1)

            def tiles(i):
                matrix_at = column(pe, 1, i, (E - 1) * D)
                turn(i, 0)
                for q in range(RB):
                    if q + 1 < RB:
                        turn(i, q + 1)
                    product(i, q, matrix_at[q])

            tiles(0)
            with pe.Fori(1, NT // RB) as i:
                tiles(i)


def kernel(x, cond_1024, L0_cond_Wx, L0_cond_Wh, L0_cond_b, L0_ffn_router_w, L0_ffn_router_b, L0_ffn_expert_w,
           L0_ffn_expert_b):
    import numpy as np
    import concourse.bacc as bacc
    from concourse.bass_utils import run_bass_kernel_spmd

    def chunks(a):
        a = np.asarray(a)
        return np.ascontiguousarray(a.reshape(KC, P, -1).transpose(1, 0, 2).reshape(P, -1))

    x = np.ascontiguousarray(x)
    xT = np.ascontiguousarray(x.reshape(P, NG, GS, KC, P).transpose(1, 4, 3, 2, 0).reshape(NG, P, KC * GW))
    arrays = {
        "xT": xT,
        "x": x,
        "cT": chunks(np.asarray(cond_1024).T),
        "Wx": chunks(L0_cond_Wx),
        "Wh": chunks(L0_cond_Wh),
        "b": chunks(np.asarray(L0_cond_b).reshape(D, 1)),
        "rwT": chunks(np.asarray(L0_ffn_router_w).T),
        "rb": np.ascontiguousarray(L0_ffn_router_b).reshape(1, E),
        "weT": chunks(np.asarray(L0_ffn_expert_w).transpose(2, 0, 1).reshape(D, E * D)),
        "be": np.ascontiguousarray(L0_ffn_expert_b).reshape(1, E * D),
    }
    nc = bacc.Bacc("TRN2", target_bir_lowering=False, num_devices=1)
    args = [nc.dram_tensor(n, a.shape, mybir.dt.from_np(a.dtype), kind="ExternalInput").ap() for n, a in arrays.items()]
    out = nc.dram_tensor("out", (P, T, D), F32, kind="ExternalOutput").ap()
    adaln_moe_kernel(nc, *args, out)
    r = run_bass_kernel_spmd(nc, [arrays], core_ids=[0])
    return r.results[0]["out"]
```

```python
from contextlib import ExitStack

import concourse.bass as bass
from concourse import mybir

F32 = mybir.dt.float32
F32R = mybir.dt.float32r
BF16 = mybir.dt.bfloat16
U32 = mybir.dt.uint32
ALU = mybir.AluOpType
ACT = mybir.ActivationFunctionType
AX = mybir.AxisListType

P = 128
T = 64
D = 256
KC = D // P
E = 8
NTOK = P * T
GS = 4
NG = T // GS
GW = GS * P
NB = 4
NI = NG // NB
CAP = NTOK + P
ROWS = E * CAP
LW = P + E
COL_L, COL_H1, COL_X = P, LW, LW + P
COL_W, COL_ID = COL_X + D, COL_X + D + 1
RW = 2 * D + 16
NT = NTOK // P + E - 1
ROUND = 1.5 * 2.0 ** 23
WARM = 7
RB = 12
NR = (NT + RB - 1) // RB
REST = NT - (NR - 1) * RB
RP = 3
H = E // 2


def later(i):
    return not (isinstance(i, int) and i == 0)


def rnn_moe_kernel(nc, xT, x, cT, Wx, Wh, b, rwT, rb, weT, be, out):
    ctx = ExitStack()
    with ctx:
        def sb(name, shape, dt=F32):
            return ctx.enter_context(nc.sbuf_tensor(name, shape, dt))

        def ps(name, shape, dt=F32):
            return ctx.enter_context(nc.psum_tensor(name, shape, dt))

        def sem(name):
            return ctx.enter_context(nc.semaphore(name))

        srt = nc.dram_tensor("sorted_rows", [ROWS, RW], F32).ap()
        out_rows = out.rearrange("n t d -> (n t) d")

        wx = sb("wx", [P, KC, D])
        wx_hi = sb("wx_hi", [P, KC, D], F32R)
        wx_lo = sb("wx_lo", [P, KC, D], F32R)
        wh = sb("wh", [P, KC, D])
        bias = sb("bias", [P, KC])
        idr = sb("idr", [P, 2 * LW])
        rb_bc = sb("rb_bc", [P, GS, E])
        we = sb("we", [P, KC, E * D])
        we_hi = [sb(f"we_hi{k}", [P, E * D], F32R) for k in range(KC)]
        we_lo = [sb(f"we_lo{k}", [P, E * D], F32R) for k in range(KC)]
        be2 = sb("be2", [2, E * D])
        be_hi = sb("be_hi", [2, E * D], F32R)
        be_full = sb("be_full", [2, E * D])
        be_parts = sb("be_parts", [2, E * D], F32R)
        ones2 = sb("ones2", [2, P], F32R)
        tri = sb("tri", [P, P], BF16)
        ones = sb("ones", [P, P], BF16)
        e_less = sb("e_less", [P, GS, E])
        pid = sb("pid", [P, 1])
        tile_back = sb("tile_back", [P, E])
        tile_on = sb("tile_on", [P, E])
        first_row = sb("first_row", [P, E])
        warm = sb("warm", [P, 2])
        idle = sb("idle", [P, 512], BF16)
        sgn = sb("sgn", [2, 1])
        ids = sb("ids", [P, T], U32)

        x_first = sb("x_first", [P, KC, GW])
        xg = [sb(f"xg{i}", [P, KC, GW]) for i in range(2)]
        x_hi = [sb(f"x_hi{i}", [P, KC, GW], F32R) for i in range(2)]
        x_lo = [sb(f"x_lo{i}", [P, KC, GW], F32R) for i in range(2)]
        h0 = sb("h0", [P, KC, P])
        hT = [sb(f"hT{i}", [P, KC, P]) for i in range(GS)]
        rows = [sb(f"rows{i}", [P, GS, RW]) for i in range(NB)]
        logit = sb("logit", [P, GS, E])
        top = sb("top", [P, GS])
        below = sb("below", [P, GS, E])
        ex = sb("ex", [P, GS, E])
        ex_sum = sb("ex_sum", [P, GS])
        at_top = sb("at_top", [P, GS, E])
        choice = sb("choice", [P, GS])
        oh = sb("oh", [P, GS, E], BF16)
        oh_sum = sb("oh_sum", [P, E])
        cum = sb("cum", [P, E], BF16)
        region = sb("region", [P, GS])
        oh_rank = sb("oh_rank", [P, GS, E])
        rank_of = sb("rank_of", [P, GS])
        slot = [sb(f"slot{i}", [P, GS], U32) for i in range(NB)]

        filler = sb("filler", [P, RW])
        frac = sb("frac", [P, E])
        scan = [sb(f"scan{i}", [P, H + E]) for i in range(4)]
        tiles_before = sb("tiles_before", [P, E])
        ended = sb("ended", [P, E])
        number = sb("number", [P, 1])
        owner = sb("owner", [P, E])
        row_if = sb("row_if", [P, E])
        own_row = sb("own_row", [P, E])
        tile_cols = sb("tile_cols", [P, 2])
        tab = sb("tab", [2, NT], U32)
        capped = sb("capped", [P, E])
        done = sb("done", [P, E])
        done_half = sb("done_half", [P, E])
        todo_row = sb("todo_row", [P, E])
        from_end = sb("from_end", [P, E])
        gap = sb("gap", [P, E])
        own_gap = sb("own_gap", [P, E])
        over = sb("over", [P, 1])
        over_at = sb("over_at", [NT, NT], BF16)
        skip = sb("skip", [P, NT - RB], U32)

        tile_in = [sb(f"tile_in{i}", [P, RW]) for i in range(RB)]
        tile_id = [sb(f"tile_id{i}", [P, 1], U32) for i in range(RB)]
        tile_out = [sb(f"tile_out{i}", [P, D]) for i in range(RB)]
        hs_hi = [sb(f"hs_hi{i}", [P, KC, P], F32R) for i in range(RP)]
        hs_lo = [sb(f"hs_lo{i}", [P, KC, P], F32R) for i in range(RP)]

        pre = [[ps(f"pre{i}{j}", [P, GW]) for j in range(KC)] for i in range(2)]
        ptr = [ps(f"ptr{i}", [P, 512]) for i in range(2)]
        pcn = ps("pcn", [P, 512])
        prk = ps("prk", [P, 512])
        p_rank = prk[:, 0:GS * E].rearrange("p (s e) -> p s e", s=GS)
        p_early = prk[:, 64:64 + E]
        p_cnt = prk[:, 72:72 + E]
        p_tab = prk[0:2, 128:128 + NT]
        p_over = prk[:, 256:256 + NT - RB]
        pt2 = [pre[1][0], pre[1][1], ptr[0]]
        py = [pre[0][0], pre[0][1], pcn]

        def acc(i, bs, s, j):
            bank = (pcn, prk)[j] if bs == 0 and s % 2 and not later(i) else pre[bs % 2][j]
            return bank[:, s * P:(s + 1) * P]

        wx_in = sem("wx_in")
        wh_in = sem("wh_in")
        b_in = sem("b_in")
        r_in = sem("r_in")
        be_in = sem("be_in")
        we_in = sem("we_in")
        x_first_in = sem("x_first_in")
        x_rest_in = sem("x_rest_in")
        xg_in = [sem(f"xg_in{i}") for i in range(2)]
        xn_in = [sem(f"xn_in{i}") for i in range(NB)]

        warm_ready = sem("warm_ready")
        g_chain = sem("g_chain")
        consts = sem("consts")
        pool_go = sem("pool_go")
        scat = [sem(f"scat{i}") for i in range(NB)]

        w_ready = sem("w_ready")
        we_ready = sem("we_ready")
        hi_ready = sem("hi_ready")
        split_ready = sem("split_ready")
        wx_done = sem("wx_done")

        pre_ready = sem("pre_ready")
        h_ready = sem("h_ready")
        tr_ready = sem("tr_ready")
        hn_ready = sem("hn_ready")

        v_chain = sem("v_chain")
        d_ready = sem("d_ready")
        e_ready = sem("e_ready")
        oh_ready = sem("oh_ready")
        sum_ready = sem("sum_ready")
        cum_ready = sem("cum_ready")
        rank_ready = sem("rank_ready")
        slots_ready = sem("slots_ready")

        filled = sem("filled")
        cnt_ready = sem("cnt_ready")
        h_chain = sem("h_chain")
        tabc_ready = sem("tabc_ready")
        tabp_ready = sem("tabp_ready")
        tab_ready = sem("tab_ready")
        over_ready = sem("over_ready")
        overp_ready = sem("overp_ready")
        skip_ready = sem("skip_ready")

        t_in = [sem(f"t_in{i}") for i in range(RB)]
        t_tr = [sem(f"t_tr{i}") for i in range(RP)]
        t_hi = [sem(f"t_hi{i}") for i in range(RP)]
        t_lo = [sem(f"t_lo{i}") for i in range(RP)]
        t_y = [sem(f"t_y{i}") for i in range(RP)]
        t_o = [sem(f"t_o{i}") for i in range(RB)]
        t_out = [sem(f"t_out{i}") for i in range(RB)]

        first = xT[0, :, :].rearrange("p (k n) -> p k n", k=KC)

        def routed(i, bs, half):
            g = NB * i + bs
            return (g, 0, GS) if half is None else (g + half, half * GS // 2, GS // 2)

        block = ctx.enter_context(nc.Block())

        def entries(eng, n, i, most, tiles=RB):
            return nc.values_load_multi_w_load_instructions(
                tab[n:n + 1, bass.ds(i * RB, tiles)], engines=[eng.engine], min_val=0, max_val=most,
                skip_runtime_bounds_check_because="the table holds nothing else")[1]

        @block.sync
        def _(sp):
            def load_group(i, bs):
                if later(i) or bs > 2:
                    sp.wait_ge(split_ready, NB * i + bs - 2)
                sp.dma_start(xg[bs % 2][:, :, :].rearrange("p k n -> p (k n)"),
                             xT[NB * i + bs, :, :]).then_inc(xg_in[bs % 2], 16)

            def load_rows(i, bs):
                if later(i):
                    sp.wait_ge(scat[bs], i * (16 * GS))
                sp.dma_start(rows[bs][:, :, COL_X:COL_X + D],
                             x[:, bass.ds((NB * i + bs) * GS, GS), :]).then_inc(xn_in[bs], 16)

            sp.dma_start(wx[:, :, :].rearrange("p k n -> p (k n)"), Wx).then_inc(wx_in, 16)
            sp.dma_start(h0[:, :, :].rearrange("p k n -> p (k n)"), cT).then_inc(wh_in, 16)
            sp.dma_start(x_first[:, :, P:GW], first[:, :, P:GW]).then_inc(x_rest_in, 16)
            load_group(0, 1)
            load_rows(0, 0)

            def body(i):
                for bs in range(0 if later(i) else 2, NB):
                    load_group(i, bs)
                    load_rows(*((i, bs - 1) if bs else (i - 1, NB - 1)))
                    if not later(i):
                        sp.wait_ge(consts, 1)
                        for e in range((bs - 2) * E // 2, (bs - 1) * E // 2):
                            sp.dma_start(srt[e * CAP:e * CAP + P, :], filler[:, :]).then_inc(filled, 16)

            body(0)
            with sp.Fori(1, NI) as i:
                body(i)
            load_rows(NI - 1, NB - 1)

            sp.wait_ge(filled, 16 * E)
            sp.wait_ge(tab_ready, 1)
            for bs in range(NB):
                sp.wait_ge(scat[bs], (NI - 1) * 16 * GS)

            def load_tiles(i, tiles=RB):
                starts = entries(sp, 0, i, ROWS - P, tiles)
                for q in range(tiles):
                    if later(i):
                        sp.wait_ge(t_o[q], i)
                    sp.dma_start(tile_in[q][:, :], srt[bass.ds(starts[q], P), :]).then_inc(t_in[q], 16)

            load_tiles(0)
            sp.wait_ge(tab_ready, 2)
            for bs in range(NB):
                sp.wait_ge(scat[bs], NI * 16 * GS)
            with sp.Fori(1, NR - 1) as i:
                load_tiles(i)
            load_tiles(NR - 1, REST)

        @block.gpsimd
        def _(pool):
            pool.memset(idle[:, :], 0.0).then_inc(warm_ready, 1)
            pool.memset(warm[:, 0:1], 0.0).then_inc(warm_ready, 1)
            pool.memset(idr[:, 0:P], 0.0).then_inc(g_chain, 1)
            pool.memset(idr[:, 2 * LW - P:2 * LW], 0.0).then_inc(g_chain, 1)
            pool.memset(tri[:, :], 1.0).then_inc(g_chain, 1)
            pool.memset(filler[:, :], 0.0).then_inc(g_chain, 1)
            pool.memset(ones[:, :], 1.0)
            pool.memset(ones2[:, :].bitcast(F32), 1.0)
            pool.memset(cum[:, :], 1.0)
            for bs in range(NB):
                pool.memset(rows[bs][:, :, COL_ID + 1:RW], 0.0)
            pool.iota(e_less[:, :, :], pattern=[[0, GS], [1, E]], base=-E, channel_multiplier=0,
                      allow_small_or_imprecise_dtypes=True)
            pool.iota(pid[:, :], pattern=[[0, 1]], base=0, channel_multiplier=1,
                      allow_small_or_imprecise_dtypes=True)
            pool.iota(sgn[:, :], pattern=[[0, 1]], base=1, channel_multiplier=-2,
                      allow_small_or_imprecise_dtypes=True)
            pool.iota(tile_back[:, :], pattern=[[CAP, E]], base=-P, channel_multiplier=-P,
                      allow_small_or_imprecise_dtypes=True)
            pool.iota(first_row[:, :], pattern=[[CAP, E]], base=P, channel_multiplier=0,
                      allow_small_or_imprecise_dtypes=True)
            pool.iota(tile_on[:, :], pattern=[[CAP, E]], base=P, channel_multiplier=P,
                      allow_small_or_imprecise_dtypes=True)
            for a in scan:
                pool.memset(a[:, 0:H], 0.0)
            pool.iota(ids[:, :], pattern=[[1, T]], base=0, channel_multiplier=T)
            pool.wait_ge(g_chain, 4)
            pool.iota(filler[:, COL_ID:COL_ID + 1].bitcast(U32), pattern=[[0, 1]], base=NTOK, channel_multiplier=0)
            for at in (0, 2 * LW - P):
                pool.affine_select(out=idr[:, at:at + P], in_=idr[:, at:at + P], compare_op=ALU.not_equal, fill=1.0,
                                   base=0, pattern=[[-1, P]], channel_multiplier=1)
            pool.affine_select(out=tri[:, :], in_=tri[:, :], compare_op=ALU.is_gt, fill=0.0,
                               base=0, pattern=[[1, P]], channel_multiplier=-1).then_inc(consts, 1)

            def scatter(i, bs, half=None):
                r, s0, n = routed(i, bs, half)
                pool.wait_ge(slots_ready, r + 1)
                pool.wait_ge(hn_ready, (NB * i + bs) * GS + s0 + n)
                pool.wait_ge(xn_in[bs], i * 16 + 16)
                pool.sem_inc(pool_go, 1)
                for s in range(s0, s0 + n):
                    pool.indirect_dma_start(
                        out=srt[:, :], out_offset=bass.IndirectOffsetOnAxis(ap=slot[bs][:, s:s + 1], axis=0),
                        in_=rows[bs][:, s, :], in_offset=None).then_inc(scat[bs], 16)

            with pool.Fori(0, NI - 1) as i:
                for bs in range(NB):
                    scatter(i, bs)
            for bs in range(NB - 1):
                scatter(NI - 1, bs)
            for half in range(2):
                scatter(NI - 1, NB - 1, half)

            last_token = pool.to_reg(NTOK - 1)

            def scatter_results(i, tiles=RB):
                for q in range(tiles):
                    pool.wait_ge(t_o[q], i + 1)
                    pool.sem_inc(pool_go, 1)
                    pool.indirect_dma_start(
                        out=out_rows, out_offset=bass.IndirectOffsetOnAxis(ap=tile_id[q][:, 0:1], axis=0),
                        in_=tile_out[q][:, :], in_offset=None,
                        bounds_check=last_token, oob_is_err=False).then_inc(t_out[q], 16)

            with pool.Fori(0, NR - 1) as i:
                scatter_results(i)
            scatter_results(NR - 1, REST)
            for q in range(RB):
                pool.wait_ge(t_out[q], 16 * (NR if q < REST else NR - 1))

        @block.scalar
        def _(act):
            act.dma_start(x_first[:, :, 0:P], first[:, :, 0:P]).then_inc(x_first_in, 16)
            act.dma_start(wh[:, :, :].rearrange("p k n -> p (k n)"), Wh).then_inc(wh_in, 16)
            act.dma_start(bias[:, :], b).then_inc(b_in, 16)
            act.wait_ge(warm_ready, 2)
            nc.scalar.activation(warm[:, 1:2], warm[:, 0:1], ACT.Tanh)
            act.dma_start(idr[:, P:P + KC * E], rwT).then_inc(r_in, 16)
            act.dma_start(rb_bc[:, :, :], bass.AP(tensor=rb.tensor, offset=rb.offset,
                                                  ap=[[0, P], [0, GS], [1, E]])).then_inc(r_in, 16)
            act.dma_start(be2[:, :], bass.AP(tensor=be.tensor, offset=be.offset,
                                             ap=[[0, 2], [1, E * D]])).then_inc(be_in, 16)
            act.dma_start(we[:, :, :].rearrange("p k m -> p (k m)"), weT).then_inc(we_in, 16)
            act.wait_ge(b_in, 16)

            def tanh(i, bs, s):
                t = NB * GS * i + GS * bs + s
                for j in range(KC):
                    act.wait_ge(pre_ready, KC * t + j + 1)
                    nc.scalar.activation(hT[s][:, j, :], acc(i, bs, s, j), ACT.Tanh,
                                         bias=bias[:, j:j + 1]).then_inc(h_ready, 1)

            def store_h(i, bs, s):
                t = NB * GS * i + GS * bs + s
                if s == 0 and later(i):
                    act.wait_ge(scat[bs], i * (16 * GS))
                act.wait_ge(tr_ready, t + 1)
                nc.scalar.copy(rows[bs][:, s, 0:COL_X], ptr[s % 2][:, 0:COL_X]).then_inc(hn_ready, 1)

            def exps(i, bs, half=None):
                r, s0, n = routed(i, bs, half)
                act.wait_ge(d_ready, r + 1)
                nc.scalar.activation(ex[:, s0:s0 + n, :], below[:, s0:s0 + n, :], ACT.Exp).then_inc(e_ready, 1)

            def body(i):
                for bs in range(NB):
                    last = (i, bs - 1) if bs else (i - 1, NB - 1)
                    for s in range(GS):
                        tanh(i, bs, s)
                        if s:
                            store_h(i, bs, s - 1)
                        elif bs or later(i):
                            store_h(*last, GS - 1)
                        if s == 1 and (bs or later(i)):
                            exps(*last)

            body(0)
            with act.Fori(1, NI) as i:
                body(i)
            exps(NI - 1, NB - 1, 0)
            store_h(NI - 1, NB - 1, GS - 1)

            def high_parts(i, q):
                qp, n = q % RP, RB // RP * i + q // RP
                act.wait_ge(t_tr[qp], n + 1)
                if q >= RP or later(i):
                    act.wait_ge(t_y[qp], n)
                nc.scalar.copy(hs_hi[qp][:, :, :].rearrange("p k n -> p (k n)"), pt2[qp][:, 0:D]).then_inc(t_hi[qp], 1)

            for q in range(RP):
                high_parts(0, q)
            exps(NI - 1, NB - 1, 1)
            for q in range(RP, RB):
                high_parts(0, q)
            with act.Fori(1, NR - 1) as i:
                for q in range(RB):
                    high_parts(i, q)
            for q in range(REST):
                high_parts(NR - 1, q)

        CHOOSE = 4
        RK = CHOOSE + 2

        @block.vector
        def _(dve):
            V = nc.vector

            dve.wait_ge(wx_in, 16)
            V.tensor_copy(wx_hi[:, :, :], wx[:, :, :]).then_inc(w_ready, 1)
            dve.wait_ge(w_ready, 1)
            V.tensor_tensor(wx_lo[:, :, :], wx[:, :, :], wx_hi[:, :, :].bitcast(F32), ALU.subtract).then_inc(w_ready, 1)

            def split(i, bs):
                g = NB * i + bs
                ring = bs % 2
                dve.wait_ge(xg_in[ring], (NB // 2 * i + bs // 2 + ring) * 16)
                if later(i) or bs > 2:
                    dve.wait_ge(wx_done, g - 2)
                V.tensor_copy(x_hi[ring][:, :, :], xg[ring][:, :, :]).then_inc(hi_ready, 1)
                dve.wait_ge(hi_ready, g)
                V.tensor_tensor(x_lo[ring][:, :, :], xg[ring][:, :, :], x_hi[ring][:, :, :].bitcast(F32),
                                ALU.subtract).then_inc(split_ready, 1)

            def route_choose(i, bs, half=None):
                r, s0, n = routed(i, bs, half)
                c = RK * r
                at = slice(s0, s0 + n)

                def over_e(a):
                    return a[:, at].rearrange("p (s o) -> p s o", o=1).to_broadcast([P, n, E])

                dve.wait_ge(hn_ready, (NB * i + bs) * GS + s0 + n)
                V.tensor_tensor(logit[:, at, :], rows[bs][:, at, COL_L:COL_L + E], rb_bc[:, at, :],
                                ALU.add).then_inc(v_chain, 1)
                dve.wait_ge(v_chain, c + 1)
                V.reduce_max(top[:, at], logit[:, at, :], AX.X).then_inc(v_chain, 1)
                dve.wait_ge(v_chain, c + 2)
                V.tensor_tensor(below[:, at, :], logit[:, at, :], over_e(top), ALU.subtract).then_inc(d_ready, 1)
                dve.wait_ge(d_ready, r + 1)
                V.scalar_tensor_tensor(out=at_top[:, at, :], in0=below[:, at, :], scalar=0.0, in1=e_less[:, at, :],
                                       op0=ALU.is_ge, op1=ALU.mult).then_inc(v_chain, 1)
                dve.wait_ge(v_chain, c + 3)
                V.tensor_reduce(choice[:, at], at_top[:, at, :], AX.X, ALU.min).then_inc(v_chain, 1)
                dve.wait_ge(v_chain, c + 4)
                V.tensor_tensor(oh[:, at, :], e_less[:, at, :], over_e(choice), ALU.is_equal).then_inc(oh_ready, 1)
                if half != 1:
                    dve.wait_ge(oh_ready, r + 1)
                    V.tensor_reduce(oh_sum[:, :], oh[:, at, :].rearrange("p s e -> p e s"), AX.X,
                                    ALU.add).then_inc(sum_ready, 1)

            def route_place(i, bs, half=None):
                r, s0, n = routed(i, bs, half)
                c = RK * r + CHOOSE
                at = slice(s0, s0 + n)
                V.tensor_scalar(region[:, at], choice[:, at], float(CAP), float(E * CAP), ALU.mult, ALU.add)
                dve.wait_ge(rank_ready, r + 1)
                V.tensor_tensor(oh_rank[:, at, :], p_rank[:, at, :], oh[:, at, :], ALU.mult).then_inc(v_chain, 1)
                dve.wait_ge(sum_ready, r + 1)
                if later(i) or bs:
                    dve.wait_ge(cum_ready, r)
                V.tensor_tensor(cum[:, :], cum[:, :], oh_sum[:, :], ALU.add).then_inc(cum_ready, 1)
                dve.wait_ge(v_chain, c + 1)
                V.reduce_sum(rank_of[:, at], oh_rank[:, at, :], AX.X)
                dve.wait_ge(e_ready, r + 1)
                V.reduce_sum(ex_sum[:, at], ex[:, at, :], AX.X).then_inc(v_chain, 1)
                dve.wait_ge(v_chain, c + 2)
                if later(i):
                    dve.wait_ge(scat[bs], i * (16 * GS))
                place(i, bs, at)

            def place(i, bs, at):
                V.tensor_tensor(slot[bs][:, at], region[:, at], rank_of[:, at], ALU.add)
                V.reciprocal(rows[bs][:, at, COL_W], ex_sum[:, at])
                V.tensor_copy(rows[bs][:, at, COL_ID].bitcast(U32),
                              ids[:, bass.ds((NB * i + bs) * GS + at.start, at.stop - at.start)]).then_inc(slots_ready, 1)

            def body(i, last=False):
                for bs in range(NB):
                    if last and bs == 2:
                        dve.wait_ge(tabp_ready, 1)
                        V.tensor_copy(tab[:, 0:RB], p_tab[:, 0:RB]).then_inc(tab_ready, 1)
                    if bs or later(i):
                        before = (i, bs - 1) if bs else (i - 1, NB - 1)
                        route_choose(*before)
                        route_place(*before)
                    if last and bs == 1:
                        early_table()
                    if bs < NB - 2:
                        split(i, bs + 2)
                    elif not last:
                        split(i + 1, bs + 2 - NB)
                    if not later(i):
                        split_bias() if bs == 0 else split_experts(bs - 1)
                    elif last and bs == 0:
                        split_experts(NB - 1)

            def split_bias():
                dve.wait_ge(be_in, 16)
                V.tensor_copy(be_hi[:, :], be2[:, :])
                V.tensor_scalar(be_full[:, :], be2[:, :], pid[0:2, 0:1], None, ALU.mult).then_inc(w_ready, 1)
                dve.wait_ge(w_ready, 3)
                V.scalar_tensor_tensor(out=be_parts[:, :], in0=be_hi[:, :].bitcast(F32), scalar=sgn[:, 0:1],
                                       in1=be_full[:, :], op0=ALU.mult, op1=ALU.add).then_inc(w_ready, 1)

            def split_experts(n):
                k, at = divmod(n * (KC * E * D // NB), E * D)
                cols = slice(at, at + KC * E * D // NB)
                if n == 0:
                    dve.wait_ge(we_in, 16)
                V.tensor_copy(we_hi[k][:, cols], we[:, k, cols]).then_inc(we_ready, 1)
                dve.wait_ge(we_ready, 2 * n + 1)
                V.tensor_tensor(we_lo[k][:, cols], we[:, k, cols], we_hi[k][:, cols].bitcast(F32),
                                ALU.subtract).then_inc(we_ready, 1)

            chain = [0]

            def link(ins, wait=True):
                chain[0] += 1
                ins.then_inc(h_chain, 1)
                if wait:
                    dve.wait_ge(h_chain, chain[0])
                return chain[0]

            whole = [a[:, H:H + E] for a in scan]
            tiles_upto = whole[3]

            def prefix(n):
                return V.tensor_tensor(whole[n + 1], whole[n], scan[n][:, H - (1 << n):H - (1 << n) + E], ALU.add)

            def shares():
                V.tensor_scalar(ended[:, :], tiles_upto, pid[:, 0:1], None, ALU.is_le)
                return V.tensor_tensor(tiles_before[:, :], tiles_upto, whole[0], ALU.subtract)

            def owners():
                V.scalar_tensor_tensor(out=owner[:, :], in0=tiles_before[:, :], scalar=pid[:, 0:1], in1=ended[:, :],
                                       op0=ALU.is_le, op1=ALU.subtract)
                V.reduce_sum(number[:, :], ended[:, :], AX.X)

            def columns():
                V.tensor_scalar(tile_cols[:, 1:2], number[:, :], float(E - 1), float(D), ALU.min, ALU.mult)
                return V.tensor_tensor(own_row[:, :], row_if[:, :], owner[:, :], ALU.mult)

            def first_rows():
                V.reduce_sum(tile_cols[:, 0:1], own_row[:, :], AX.X).then_inc(tabc_ready, 1)

            def early_table():
                dve.wait_ge(cnt_ready, 1)
                link(V.tensor_scalar(frac[:, :], p_early, 1.0 / P, (3 * P - 1) / (2.0 * P), ALU.mult, ALU.subtract))
                link(V.tensor_scalar(whole[0], frac[:, :], ROUND, ROUND, ALU.add, ALU.subtract))
                for n in range(3):
                    link(prefix(n))
                link(shares())
                owners()
                link(V.scalar_tensor_tensor(out=row_if[:, :], in0=tiles_before[:, :], scalar=float(-P), in1=tile_on[:, :],
                                            op0=ALU.mult, op1=ALU.add))
                link(columns())
                first_rows()
                link(V.tensor_scalar(capped[:, :], tiles_upto, float(RB), None, ALU.min))
                link(V.scalar_tensor_tensor(out=done[:, :], in0=tiles_before[:, :], scalar=float(RB), in1=capped[:, :],
                                            op0=ALU.min, op1=ALU.subtract))
                link(V.tensor_scalar(done_half[:, :], done[:, :], -1.0, (P + 1) / (2.0 * P), ALU.mult, ALU.add))
                link(V.scalar_tensor_tensor(out=todo_row[:, :], in0=done[:, :], scalar=float(-P), in1=first_row[:, :],
                                            op0=ALU.mult, op1=ALU.add))

            def last_rows_and_late_table():
                r, s0, n = routed(NI - 1, NB - 1, 1)
                at = slice(s0, s0 + n)
                c = RK * r + CHOOSE
                V.tensor_scalar(region[:, at], choice[:, at], float(CAP), float(E * CAP), ALU.mult, ALU.add)
                dve.wait_ge(rank_ready, r + 1)
                V.tensor_tensor(oh_rank[:, at, :], p_rank[:, at, :], oh[:, at, :], ALU.mult).then_inc(v_chain, 1)
                dve.wait_ge(cnt_ready, 2)
                V.tensor_tensor(from_end[:, :], p_cnt, tile_back[:, :], ALU.add)
                t = link(V.scalar_tensor_tensor(out=frac[:, :], in0=p_cnt, scalar=1.0 / P, in1=done_half[:, :],
                                                op0=ALU.mult, op1=ALU.subtract), wait=False)
                dve.wait_ge(v_chain, c + 1)
                V.reduce_sum(rank_of[:, at], oh_rank[:, at, :], AX.X)
                dve.wait_ge(e_ready, r + 1)
                V.reduce_sum(ex_sum[:, at], ex[:, at, :], AX.X).then_inc(v_chain, 1)
                dve.wait_ge(h_chain, t)
                t = link(V.tensor_scalar(whole[0], frac[:, :], ROUND, ROUND, ALU.add, ALU.subtract), wait=False)
                dve.wait_ge(v_chain, c + 2)
                place(NI - 1, NB - 1, at)
                dve.wait_ge(h_chain, t)
                t = link(prefix(0), wait=False)
                finish(0, 0)
                dve.wait_ge(h_chain, t)
                t = link(prefix(1), wait=False)
                low_parts(0, 3)
                dve.wait_ge(h_chain, t)
                t = link(prefix(2), wait=False)
                finish(0, 1)
                dve.wait_ge(h_chain, t)
                t = link(shares(), wait=False)
                low_parts(0, 4)
                dve.wait_ge(h_chain, t)
                owners()
                t = link(V.scalar_tensor_tensor(out=row_if[:, :], in0=tiles_before[:, :], scalar=float(P),
                                                in1=from_end[:, :], op0=ALU.mult, op1=ALU.add), wait=False)
                finish(0, 2)
                dve.wait_ge(h_chain, t)
                V.tensor_tensor(gap[:, :], todo_row[:, :], row_if[:, :], ALU.subtract)
                link(columns())
                first_rows()
                t = link(V.tensor_tensor(own_gap[:, :], gap[:, :], owner[:, :], ALU.mult), wait=False)
                low_parts(0, 5)
                dve.wait_ge(h_chain, t)
                link(V.reduce_sum(over[:, :], own_gap[:, :], AX.X))
                V.tensor_scalar(over_at[:, :], idr[0:NT, 0:NT], over[0:NT, 0:1], None, ALU.mult).then_inc(over_ready, 1)
                dve.wait_ge(tabp_ready, 2)
                V.tensor_copy(tab[:, RB:NT], p_tab[:, RB:NT]).then_inc(tab_ready, 1)
                finish(0, 3)
                low_parts(0, 6)
                dve.wait_ge(overp_ready, 1)
                V.tensor_scalar(skip[:, :], p_over, pid[:, 0:1], float(NTOK), ALU.is_gt, ALU.mult).then_inc(skip_ready, 1)

            split(0, 1)
            dve.wait_ge(consts, 1)
            dve.wait_ge(r_in, 32)
            body(0)
            with dve.Fori(1, NI - 1) as i:
                body(i)
            body(NI - 1, last=True)
            route_choose(NI - 1, NB - 1, 0)
            route_place(NI - 1, NB - 1, 0)

            def low_parts(i, q):
                qp, n = q % RP, RB // RP * i + q // RP
                if q >= RP or later(i):
                    dve.wait_ge(t_y[qp], n)
                dve.wait_ge(t_hi[qp], n + 1)
                V.tensor_tensor(hs_lo[qp][:, :, :].rearrange("p k n -> p (k n)"), pt2[qp][:, 0:D],
                                hs_hi[qp][:, :, :].rearrange("p k n -> p (k n)").bitcast(F32),
                                ALU.subtract).then_inc(t_lo[qp], 1)

            def finish(i, q):
                qp, n = q % RP, RB // RP * i + q // RP
                if later(i):
                    dve.wait_ge(t_out[q], i * 16)
                dve.wait_ge(t_y[qp], n + 1)
                ids_in = tile_in[q][:, COL_ID:COL_ID + 1].bitcast(U32)
                if later(i):
                    V.tensor_tensor(tile_id[q][:, :], ids_in, skip[:, bass.ds((i - 1) * RB + q, 1)], ALU.max)
                else:
                    V.tensor_copy(tile_id[q][:, :], ids_in)
                V.scalar_tensor_tensor(out=tile_out[q][:, :], in0=py[qp][:, 0:D],
                                       scalar=tile_in[q][:, COL_W:COL_W + 1],
                                       in1=tile_in[q][:, COL_X:COL_X + D],
                                       op0=ALU.mult, op1=ALU.add).then_inc(t_o[q], 1)

            low_parts(0, 0)
            low_parts(0, 1)
            route_choose(NI - 1, NB - 1, 1)
            low_parts(0, 2)
            last_rows_and_late_table()
            for q in range(4, RB):
                finish(0, q)
                if q + RP < RB:
                    low_parts(0, q + RP)

            def tiles_of_round(i, tiles=RB):
                low_parts(i, 0)
                for q in range(tiles):
                    if q + 1 < tiles:
                        low_parts(i, q + 1)
                    finish(i, q)

            dve.wait_ge(skip_ready, 1)
            with dve.Fori(1, NR - 1) as i:
                tiles_of_round(i)
            tiles_of_round(NR - 1, REST)

        @block.tensor
        def _(pe):
            mm = nc.tensor.matmul

            def project_first(s):
                cols = slice(s * P, (s + 1) * P)
                for j in range(KC):
                    for k in range(KC):
                        mm(acc(0, 0, s, j), wx[:, k, j * P:(j + 1) * P], x_first[:, k, cols],
                           start=(k == 0), stop=False, skip_group_check=True)

            def project(ring, s):
                j, k = s // KC, s % KC
                cols = slice(j * P, (j + 1) * P)
                mm(pre[ring][j][:, :], wx_hi[:, k, cols], x_hi[ring][:, k, :], start=(k == 0), stop=False,
                   skip_group_check=True)
                mm(pre[ring][j][:, :], wx_lo[:, k, cols], x_hi[ring][:, k, :], start=False, stop=False,
                   skip_group_check=True)
                last = mm(pre[ring][j][:, :], wx_hi[:, k, cols], x_lo[ring][:, k, :], start=False, stop=False,
                          skip_group_check=True)
                if s == GS - 1:
                    last.then_inc(wx_done, 1)

            def recur(i, bs, s, first=False):
                t = NB * GS * i + GS * bs + s
                old = h0 if first else hT[(s - 1) % GS]
                for j in range(KC):
                    for k in range(KC):
                        if j == 0 and not first:
                            pe.wait_ge(h_ready, KC * t - 1 + k)
                        last = mm(acc(i, bs, s, j), wh[:, k, j * P:(j + 1) * P], old[:, k, :],
                                  start=False, stop=(k == KC - 1), skip_group_check=True)
                    last.then_inc(pre_ready, 1)

            def after(i, bs, s):
                t = NB * GS * i + GS * bs + s
                if later(i) or bs or s > 1:
                    pe.wait_ge(hn_ready, t - 1)
                for k in range(KC):
                    last = mm(ptr[s % 2][:, k * P:k * P + LW], hT[s][:, k, :], idr[:, k * LW:(k + 1) * LW],
                              start=(k == 0), stop=(k == KC - 1), skip_group_check=True)
                last.then_inc(tr_ready, 1)

            def rank(i, bs, half=None, counts=None):
                r, s0, n = routed(i, bs, half)
                end = s0 + n
                pe.wait_ge(oh_ready, r + 1)
                if counts == "early":
                    pe.wait_ge(cum_ready, r)
                    mm(p_early, ones[:, :], cum[:, :], start=True, stop=True,
                       skip_group_check=True).then_inc(cnt_ready, 1)
                elif counts == "all":
                    for s in range(s0, end):
                        mm(p_cnt, ones[:, :], oh[:, s, :], start=(s == s0), stop=False, skip_group_check=True)
                    pe.wait_ge(cum_ready, r)
                    mm(p_cnt, ones[:, :], cum[:, :], start=False, stop=True, skip_group_check=True).then_inc(cnt_ready, 1)
                mm(p_rank[:, s0:end, :], tri[:, :], oh[:, s0:end, :], start=True, stop=False, skip_group_check=True)
                for s in range(s0, end - 1):
                    mm(p_rank[:, s + 1:end, :], ones[:, :],
                       oh[:, s, :].rearrange("p (o e) -> p o e", o=1).to_broadcast([P, end - 1 - s, E]),
                       start=False, stop=False, skip_group_check=True)
                if later(i) or bs:
                    pe.wait_ge(cum_ready, r)
                mm(p_rank[:, s0:end, :], ones[:, :], cum[:, :].rearrange("p (o e) -> p o e", o=1).to_broadcast([P, n, E]),
                   start=False, stop=True, skip_group_check=True).then_inc(rank_ready, 1)

            def body(i, last=False):
                for bs in range(NB):
                    before = (i, bs - 1) if bs else (i - 1, NB - 1)
                    started = bs > 0 or later(i)
                    for s in range(GS):
                        recur(i, bs, s, first=not started and s == 0)
                        late = last and bs == NB - 1
                        if late and s == 2:
                            rank(*before)
                        if not started and s + 1 < GS:
                            if s == 0:
                                pe.wait_ge(x_rest_in, 16)
                            project_first(s + 1)
                        if s:
                            if not started and s == 1:
                                pe.wait_ge(consts, 1)
                                pe.wait_ge(r_in, 32)
                            after(i, bs, s - 1)
                        elif started:
                            after(*before, GS - 1)
                        if not late:
                            if s == (0 if started else 1):
                                pe.wait_ge(split_ready, NB * i + bs + 1)
                            for part in (s,) if started else ((), (0,), (1,), (2, 3))[s]:
                                project(1 - bs % 2, part)
                        if s == 1 and started and not late:
                            rank(*before, counts="early" if last and bs == 1 else None)
                        if last and bs == 2 and s == 0:
                            pe.wait_ge(tabc_ready, 1)
                            mm(p_tab[:, 0:RB], tile_cols[:, :], idr[:, 0:RB], start=True, stop=True,
                               skip_group_check=True).then_inc(tabp_ready, 1)

            pe.wait_ge(warm_ready, 1)
            for n in range(WARM):
                mm(prk[:, :], idle[:, 0:P], idle[:, :], start=True, stop=True, skip_group_check=True)
            pe.wait_ge(wx_in, 16)
            pe.wait_ge(x_first_in, 16)
            project_first(0)
            pe.wait_ge(wh_in, 32)
            body(0)
            with pe.Fori(1, NI - 1) as i:
                body(i)
            body(NI - 1, last=True)
            pe.wait_ge(h_ready, KC * T)
            after(NI - 1, NB - 1, GS - 1)
            rank(NI - 1, NB - 1, 0)

            def turn(i, q):
                qp, n = q % RP, RB // RP * i + q // RP
                pe.wait_ge(t_in[q], i * 16 + 16)
                if q >= RP or later(i):
                    pe.wait_ge(t_lo[qp], n)
                for k in range(KC):
                    last = nc.tensor.transpose(pt2[qp][:, k * P:(k + 1) * P], tile_in[q][:, k * LW:k * LW + P], idr[:, 0:P])
                last.then_inc(t_tr[qp], 1)

            def product(i, q, at):
                qp, n = q % RP, RB // RP * i + q // RP
                cols = bass.ds(at, D)
                if q >= RP:
                    pe.wait_ge(t_o[q - RP], i + 1)
                elif later(i):
                    pe.wait_ge(t_o[q + RB - RP], i)
                mm(py[qp][:, 0:D], ones2[:, :], be_parts[:, cols], start=True, stop=False, skip_group_check=True)
                pe.wait_ge(t_hi[qp], n + 1)
                for k in range(KC):
                    mm(py[qp][:, 0:D], hs_hi[qp][:, k, :], we_hi[k][:, cols], start=False, stop=False, skip_group_check=True)
                    mm(py[qp][:, 0:D], hs_hi[qp][:, k, :], we_lo[k][:, cols], start=False, stop=False, skip_group_check=True)
                pe.wait_ge(t_lo[qp], n + 1)
                for k in range(KC):
                    last = mm(py[qp][:, 0:D], hs_lo[qp][:, k, :], we_hi[k][:, cols], start=False, stop=(k == KC - 1),
                              skip_group_check=True)
                last.then_inc(t_y[qp], 1)

            pe.wait_ge(tab_ready, 1)
            matrix_at = entries(pe, 1, 0, (E - 1) * D)
            pe.wait_ge(hn_ready, T)
            for q in range(RP):
                turn(0, q)
            pe.wait_ge(w_ready, 4)
            pe.wait_ge(we_ready, 2 * NB)
            for q in range(5):
                product(0, q, matrix_at[q])
                turn(0, q + RP)
                if q == 1:
                    rank(NI - 1, NB - 1, 1, counts="all")
            pe.wait_ge(tabc_ready, 2)
            mm(p_tab[:, RB:NT], tile_cols[:, :], idr[:, 0:NT - RB], start=True, stop=True,
               skip_group_check=True).then_inc(tabp_ready, 1)
            pe.wait_ge(tab_ready, 2)
            pe.wait_ge(over_ready, 1)
            mm(p_over, ones[0:NT, :], over_at[:, 0:NT - RB], start=True, stop=True,
               skip_group_check=True).then_inc(overp_ready, 1)
            for q in range(5, RB):
                product(0, q, matrix_at[q])
                if q + RP < RB:
                    turn(0, q + RP)

            def tiles_of_round(i, tiles=RB):
                matrix_at = entries(pe, 1, i, (E - 1) * D, tiles)
                turn(i, 0)
                for q in range(tiles):
                    if q + 1 < tiles:
                        turn(i, q + 1)
                    product(i, q, matrix_at[q])

            with pe.Fori(1, NR - 1) as i:
                tiles_of_round(i)
            tiles_of_round(NR - 1, REST)


def kernel(x, cond_1024, L0_cond_Wx, L0_cond_Wh, L0_cond_b, L0_ffn_router_w, L0_ffn_router_b, L0_ffn_expert_w,
           L0_ffn_expert_b):
    import numpy as np
    import concourse.bacc as bacc
    from concourse.bass_utils import run_bass_kernel_spmd

    def chunks(a):
        a = np.asarray(a)
        return np.ascontiguousarray(a.reshape(KC, P, -1).transpose(1, 0, 2).reshape(P, -1))

    x = np.ascontiguousarray(x)
    xT = np.ascontiguousarray(x.reshape(P, NG, GS, KC, P).transpose(1, 4, 3, 2, 0).reshape(NG, P, KC * GW))
    arrays = {
        "xT": xT,
        "x": x,
        "cT": chunks(np.asarray(cond_1024).T),
        "Wx": chunks(L0_cond_Wx),
        "Wh": chunks(L0_cond_Wh),
        "b": chunks(np.asarray(L0_cond_b).reshape(D, 1)),
        "rwT": chunks(np.asarray(L0_ffn_router_w).T),
        "rb": np.ascontiguousarray(L0_ffn_router_b).reshape(1, E),
        "weT": chunks(np.asarray(L0_ffn_expert_w).transpose(2, 0, 1).reshape(D, E * D)),
        "be": np.ascontiguousarray(L0_ffn_expert_b).reshape(1, E * D),
    }
    nc = bacc.Bacc("TRN2", target_bir_lowering=False, num_devices=1)
    args = [nc.dram_tensor(n, a.shape, mybir.dt.from_np(a.dtype), kind="ExternalInput").ap() for n, a in arrays.items()]
    out = nc.dram_tensor("out", (P, T, D), F32, kind="ExternalOutput").ap()
    rnn_moe_kernel(nc, *args, out)
    r = run_bass_kernel_spmd(nc, [arrays], core_ids=[0])
    return r.results[0]["out"]
```
